# Optimizing a Trainium2 kernel written in Bass

```python
import numpy as np
import jax
import jax.numpy as jnp

def _softmax(x, axis=-1):
    return jax.nn.softmax(x, axis=axis)

def _gelu(x):
    return jax.nn.gelu(x, approximate=True)

def _silu(x):
    return jax.nn.silu(x)

def _sigmoid(x):
    return jax.nn.sigmoid(x)

def _layernorm(x, axis=-1, eps=1e-05):
    m = jnp.mean(x, axis=axis, keepdims=True)
    v = jnp.var(x, axis=axis, keepdims=True)
    return (x - m) / jnp.sqrt(v + eps)

def _scatter_add(tgt, idx, src, axis=0):
    return tgt.at[idx].add(src)

def _segment_sum(src, seg, n):
    return jax.ops.segment_sum(src, seg, n)
kernel_name = 'mk_seq_preln_d1_jaxref_r4_ff293b'

def setup_inputs(seed: int=0):
    np.random.seed(seed)
    _w = jnp.asarray

    def _L0_attn_setup():
        import jax, jax.numpy as jnp
        import numpy as np
        D_MODEL = 256
        N_HEADS = 16
        CHUNK = 64
        EPS = 1e-06

        def elu_plus_1(x):
            return jax.nn.elu(x) + 1.0
        key = jax.random.key(seed)
        kx, kq, kk, kv, ko = jax.random.split(key, 5)
        B, T = (4, 1024)
        lim = float(np.sqrt(6.0 / (D_MODEL + D_MODEL)))
        mk = lambda k: jax.random.uniform(k, (D_MODEL, D_MODEL), jnp.float32, -lim, lim)
        return {'x': jax.random.normal(kx, (B, T, D_MODEL), jnp.float32), 'W_q': mk(kq), 'W_k': mk(kk), 'W_v': mk(kv), 'W_o': mk(ko)}
    _L0_attn_in = _L0_attn_setup()

    def _L0_ffn_setup():
        import jax, jax.numpy as jnp
        import numpy as np
        DIM = 256

        def _reference_tuple_inner(x, W_r, W_k, W_v, mu_r, mu_k):
            B, T, C = x.shape
            x_prev = jnp.concatenate([jnp.zeros((B, 1, C), x.dtype), x[:, :-1, :]], axis=1)
            xr = mu_r * x + (1.0 - mu_r) * x_prev
            xk = mu_k * x + (1.0 - mu_k) * x_prev
            r = jax.nn.sigmoid(jnp.einsum('btc,dc->btd', xr, W_r))
            k = jnp.einsum('btc,dc->btd', xk, W_k)
            k_act = jnp.square(jax.nn.relu(k))
            out = r * jnp.einsum('btc,dc->btd', k_act, W_v)
            new_state = x[:, -1, :]
            return (out, new_state)
        key = jax.random.key(seed)
        ks = jax.random.split(key, 6)
        B, T, C = (8, 512, DIM)
        x = jax.random.normal(ks[0], (B, T, C), dtype=jnp.float32)
        s = 1.0 / np.sqrt(C)
        W_r = jax.random.uniform(ks[1], (C, C), jnp.float32, -s, s)
        W_k = jax.random.uniform(ks[2], (C, C), jnp.float32, -s, s)
        W_v = jax.random.uniform(ks[3], (C, C), jnp.float32, -s, s)
        mu_r = jax.random.uniform(ks[4], (C,), jnp.float32)
        mu_k = jax.random.uniform(ks[5], (C,), jnp.float32)
        return {'x': x, 'W_r': W_r, 'W_k': W_k, 'W_v': W_v, 'mu_r': mu_r, 'mu_k': mu_k}
    _L0_ffn_in = _L0_ffn_setup()
    _d = {'L0_attn_x': _L0_attn_in['x'], 'L0_attn_W_q': _L0_attn_in['W_q'], 'L0_attn_W_k': _L0_attn_in['W_k'], 'L0_attn_W_v': _L0_attn_in['W_v'], 'L0_attn_W_o': _L0_attn_in['W_o'], 'L0_ffn_W_r': _L0_ffn_in['W_r'], 'L0_ffn_W_k': _L0_ffn_in['W_k'], 'L0_ffn_W_v': _L0_ffn_in['W_v'], 'L0_ffn_mu_r': _L0_ffn_in['mu_r'], 'L0_ffn_mu_k': _L0_ffn_in['mu_k']}
    _x0 = _d['L0_attn_x']
    _d['L0_attn_x'] = jax.random.normal(jax.random.fold_in(jax.random.key(seed), 1), (16, 1024, 256), dtype=_x0.dtype)
    del _x0
    return _d

def reference(L0_attn_x, L0_attn_W_q, L0_attn_W_k, L0_attn_W_v, L0_attn_W_o, L0_ffn_W_r, L0_ffn_W_k, L0_ffn_W_v, L0_ffn_mu_r, L0_ffn_mu_k):

    def _L0_attn_ref(x, W_q, W_k, W_v, W_o):
        import jax, jax.numpy as jnp
        import numpy as np
        D_MODEL = 256
        N_HEADS = 16
        CHUNK = 64
        EPS = 1e-06

        def elu_plus_1(x):
            return jax.nn.elu(x) + 1.0
        B, T, D = x.shape
        H = N_HEADS
        dk = D // H
        dv = dk
        C = CHUNK
        N = T // C
        q = (x @ W_q.T).reshape(B, T, H, dk)
        k = (x @ W_k.T).reshape(B, T, H, dk)
        v = (x @ W_v.T).reshape(B, T, H, dv)
        phi_q = elu_plus_1(q).reshape(B, N, C, H, dk)
        phi_k = elu_plus_1(k).reshape(B, N, C, H, dk)
        vc = v.reshape(B, N, C, H, dv)
        KV = jnp.einsum('bnchk,bnchv->bnhkv', phi_k, vc)
        Ksum = phi_k.sum(axis=2)
        KV_cum = jnp.cumsum(KV, axis=1)
        Ksum_cum = jnp.cumsum(Ksum, axis=1)
        S_prefix = jnp.concatenate([jnp.zeros_like(KV_cum[:, :1]), KV_cum[:, :-1]], axis=1)
        z_prefix = jnp.concatenate([jnp.zeros_like(Ksum_cum[:, :1]), Ksum_cum[:, :-1]], axis=1)
        inter = jnp.einsum('bnchk,bnhkv->bnchv', phi_q, S_prefix)
        z_inter = jnp.einsum('bnchk,bnhk->bnch', phi_q, z_prefix)
        mask = jnp.tril(jnp.ones((C, C), dtype=x.dtype))
        attn = jnp.einsum('bnihk,bnjhk->bnhij', phi_q, phi_k) * mask
        intra = jnp.einsum('bnhij,bnjhv->bnihv', attn, vc)
        z_intra = attn.sum(axis=-1).transpose(0, 1, 3, 2)
        denom = jnp.clip((z_inter + z_intra)[..., None], 1e-06, None)
        y = (inter + intra) / denom
        y = y.reshape(B, T, H * dv)
        return y @ W_o.T

    def _L0_ffn_ref(x, W_r, W_k, W_v, mu_r, mu_k):
        import jax, jax.numpy as jnp
        import numpy as np
        DIM = 256

        def _reference_tuple_inner(x, W_r, W_k, W_v, mu_r, mu_k):
            B, T, C = x.shape
            x_prev = jnp.concatenate([jnp.zeros((B, 1, C), x.dtype), x[:, :-1, :]], axis=1)
            xr = mu_r * x + (1.0 - mu_r) * x_prev
            xk = mu_k * x + (1.0 - mu_k) * x_prev
            r = jax.nn.sigmoid(jnp.einsum('btc,dc->btd', xr, W_r))
            k = jnp.einsum('btc,dc->btd', xk, W_k)
            k_act = jnp.square(jax.nn.relu(k))
            out = r * jnp.einsum('btc,dc->btd', k_act, W_v)
            new_state = x[:, -1, :]
            return (out, new_state)
        return _reference_tuple_inner(x, W_r, W_k, W_v, mu_r, mu_k)[0]
    x = L0_attn_x
    x = x + _L0_attn_ref(_layernorm(x, axis=-1), L0_attn_W_q, L0_attn_W_k, L0_attn_W_v, L0_attn_W_o)
    x = x + _L0_ffn_ref(_layernorm(x, axis=-1), L0_ffn_W_r, L0_ffn_W_k, L0_ffn_W_v, L0_ffn_mu_r, L0_ffn_mu_k)
    return x

_drawn_inputs = setup_inputs


def setup_inputs(seed=0):
    import zlib

    import numpy as np

    out = dict(_drawn_inputs(seed))
    spreads = {}
    factors = {'L0_attn_W_q': 5.237, 'L0_attn_W_k': 2.883, 'L0_ffn_W_r': 3.171, 'L0_ffn_mu_r': 6.404}
    for name, (base, spread) in spreads.items():
        noise = np.random.default_rng([zlib.crc32(name.encode()), seed]).standard_normal(out[name].shape)
        drawn = base * np.exp(spread * noise) if base else spread * noise
        out[name] = jnp.asarray(drawn.astype(out[name].dtype))
    for name, factor in factors.items():
        out[name] = (out[name] * factor).astype(out[name].dtype)
    return out
```

```python
from contextlib import ExitStack

import concourse.bass as bass
from concourse import mybir

F32 = mybir.dt.float32
F32R = mybir.dt.float32r
ACT = mybir.ActivationFunctionType
ALU = mybir.AluOpType

P = 128
HEADS = 16
DH = 16
VW = DH + 1
PAIRS = HEADS // 2
CHUNK = 64
TILES = 2
MACRO = TILES * P
LN_EPS = 1e-5
DEN_MIN = 1e-6
UNROLL = 4
FIRST = 3


def ahead(n):
    return not isinstance(n, int) or n > 0


def build(nc, x, w_q, w_k, w_v, w_o, f_r, f_k, f_v, mu_r, mu_k, out):
    B, T, D = x.shape
    KB = D // P
    MACROS = B * T // MACRO
    assert T // MACRO == UNROLL and D == HEADS * DH == 2 * P
    x_m = x.rearrange("b (m t p) c -> (b m) p t c", t=TILES, p=P)
    out_m = out.rearrange("b (m t p) c -> (b m) p t c", t=TILES, p=P)

    ctx = ExitStack()
    with ctx:
        def sb(name, shape, dt=F32):
            return ctx.enter_context(nc.sbuf_tensor(name, shape, dt))

        def sem(name):
            return ctx.enter_context(nc.semaphore(name))

        ident = sb("ident", [P, P])
        diagonals = sb("diagonals", [P, 2, CHUNK])
        causal = sb("causal", [P, CHUNK])
        head_pick = sb("head_pick", [P, 4])
        par_mask = sb("par_mask", [P, 2])
        slot_mask = sb("slot_mask", [P, 2])
        pair_mask = sb("pair_mask", [P, 4])
        zero_state = sb("zero_state", [P, KB, 2, 4 * VW])
        zero_col = sb("zero_col", [P, KB, 1])
        minus_half = sb("minus_half", [P, TILES])
        mu_r_sb = sb("mu_r_sb", [P, KB])
        mu_k_sb = sb("mu_k_sb", [P, KB])

        NW = 7
        w_nat = sb("w_nat", [P, NW, KB, D])
        w_o_sorted = sb("w_o_sorted", [P, KB, 2, PAIRS, DH])
        w_hi = sb("w_hi", [P, NW, KB, D], F32R)
        w_lo = sb("w_lo", [P, NW, KB, D], F32R)
        WQ, WK, WV, WO, FR, FK, FV = range(NW)

        x_sb = sb("x_sb", [P, 4, TILES, D])
        stats1 = sb("stats1", [P, TILES, 6])
        mv1 = sb("mv1", [P, TILES, 2])
        ve1 = sb("ve1", [P, TILES])
        rstd1 = sb("rstd1", [P, TILES])
        xn1 = sb("xn1", [P, TILES, D])
        xT_hi = sb("xT_hi", [P, KB, MACRO], F32R)
        xT_lo = sb("xT_lo", [P, KB, MACRO], F32R)
        q_relu = sb("q_relu", [P, KB, MACRO])
        q_exp = sb("q_exp", [P, KB, MACRO])
        k_relu = sb("k_relu", [P, KB, MACRO])
        k_exp = sb("k_exp", [P, KB, MACRO])
        phi_q = sb("phi_q", [P, KB, MACRO])
        phi_k = sb("phi_k", [P, KB, MACRO])
        q_par = sb("q_par", [P, 2, KB, 2 * TILES, 2, CHUNK])
        k_slot = sb("k_slot", [P, 2, KB, 2 * TILES, 2, CHUNK])
        v_state = sb("v_state", [P, 2, TILES, 2, HEADS, VW])
        v_pair = sb("v_pair", [P, 2, 2, TILES, 4, 2, 2, VW])

        k_par = sb("k_par", [P, 2, 2, TILES, D])
        probs = sb("probs", [P, TILES, 2, 2, KB, 2, CHUNK])
        kv_own = sb("kv_own", [P, TILES, KB, 2, 4 * VW])
        state = sb("state", [P, TILES, KB, 2, 4 * VW])
        den = sb("den", [P, TILES, HEADS])
        rden = sb("rden", [P, TILES, HEADS])
        yn = sb("yn", [P, TILES, HEADS, DH])
        yT_hi = sb("yT_hi", [P, 2, MACRO], F32R)
        yT_lo = sb("yT_lo", [P, 2, MACRO], F32R)

        x2 = sb("x2", [P, 2, TILES, D])
        stats2 = sb("stats2", [P, TILES, 6])
        mv2 = sb("mv2", [P, TILES, 2])
        ve2 = sb("ve2", [P, TILES])
        rstd2 = sb("rstd2", [P, TILES])
        xn2 = sb("xn2", [P, TILES, D])
        wait_carrier = sb("wait_carrier", [P, 1])
        x2T = sb("x2T", [P, 2, KB, 1 + MACRO])
        shift = sb("shift", [P, KB, MACRO])
        xk = sb("xk", [P, KB, MACRO])
        xr = sb("xr", [P, KB, MACRO])
        xk_hi = sb("xk_hi", [P, KB, MACRO], F32R)
        xk_lo = sb("xk_lo", [P, KB, MACRO], F32R)
        xr_hi = sb("xr_hi", [P, KB, MACRO], F32R)
        xr_lo = sb("xr_lo", [P, KB, MACRO], F32R)
        relu_k = sb("relu_k", [P, KB, MACRO])
        act_k = sb("act_k", [P, KB, MACRO])
        act_hi = sb("act_hi", [P, KB, MACRO], F32R)
        act_lo = sb("act_lo", [P, KB, MACRO], F32R)
        tanh_r = sb("tanh_r", [P, TILES, D])
        gated = sb("gated", [P, TILES, D])
        out_sb = sb("out_sb", [P, 2, TILES, D])

        bank = [ctx.enter_context(nc.psum_tensor(f"bank{i}", [P, 512], F32)) for i in range(4)]
        bank_scores = ctx.enter_context(nc.psum_tensor("bank_scores", [P, 2, 512], F32))
        bank_y = ctx.enter_context(nc.psum_tensor("bank_y", [P, 512], F32))
        bank_kv = ctx.enter_context(nc.psum_tensor("bank_kv", [P, 512], F32))
        turn_banks = [bank[1][:, :], bank[2][:, :], bank[3][:, :], bank_y[:, :], bank_kv[:, :],
                      bank_scores[:, 0], bank_scores[:, 1]]
        ps_w = [b.rearrange("p (a n) -> p a n", a=KB) for b in turn_banks]
        EARLY, LATE = (WQ, WK, WV), (WO, FR, FK, FV)
        feat = [b[:, :].rearrange("p (a n) -> p a n", a=KB) for b in bank]
        ps_xT, ps_q, ps_k = feat[0], feat[1], feat[2]
        ps_ktok = bank[3][:, :].rearrange("p (t n) -> p t n", t=TILES)
        ps_v = ps_ktok
        ps_fk = feat[1]
        ps_r = bank[2][:, :].rearrange("p (t n) -> p t n", t=TILES)
        ps_wo = bank_y[:, :].rearrange("p (t n) -> p t n", t=TILES)
        ps_fo = bank_kv[:, :].rearrange("p (t n) -> p t n", t=TILES)
        ps_y = bank_y[:, 0:HEADS * VW].rearrange("p (g w) -> p g w", w=VW)
        ps_kv = bank_kv[:, 0:4 * VW].rearrange("p (b n) -> p b n", b=KB)

        ident_ready = sem("ident_ready")
        const_ready = sem("const_ready")
        picks_ready = sem("picks_ready")
        v_init = sem("v_init")
        mu_in = sem("mu_in")
        w_in = [sem(f"w_in{n}") for n in range(NW)]
        w_turned = sem("w_turned")
        masks_ready = sem("masks_ready")
        w_o_ready = sem("w_o_ready")
        w_hi_ready = sem("w_hi_ready")
        w_ready = sem("w_ready")
        x_in = [sem(f"x_in{n}") for n in range(4)]
        out_stored = [sem(f"out_stored{n}") for n in range(2)]
        pe_xT = sem("pe_xT")
        pe_scores = sem("pe_scores")
        pe_ktok = sem("pe_ktok")
        pe_q = sem("pe_q")
        pe_wo = sem("pe_wo")
        pe_k = sem("pe_k")
        pe_kv = sem("pe_kv")
        pe_v = sem("pe_v")
        pe_y = sem("pe_y")
        pe_x2T = sem("pe_x2T")
        pe_fk = sem("pe_fk")
        pe_yT = sem("pe_yT")
        pe_r = sem("pe_r")
        pe_fo = sem("pe_fo")
        xT_hi_ready = sem("xT_hi_ready")
        k_par_ready = sem("k_par_ready")
        q_raw_ready = sem("q_raw_ready")
        k_raw_ready = sem("k_raw_ready")
        v_ready = sem("v_ready")
        x2T_ready = sem("x2T_ready")
        xk_hi_ready = sem("xk_hi_ready")
        xr_hi_ready = sem("xr_hi_ready")
        relu_k_ready = sem("relu_k_ready")
        act_hi_ready = sem("act_hi_ready")
        yT_hi_ready = sem("yT_hi_ready")
        tanh_ready = sem("tanh_ready")
        stats1_ready = sem("stats1_ready")
        mv1_ready = sem("mv1_ready")
        ve1_ready = sem("ve1_ready")
        xn1_ready = sem("xn1_ready")
        xT_lo_ready = sem("xT_lo_ready")
        probs_ready = sem("probs_ready")
        phi_q_ready = sem("phi_q_ready")
        phi_k_ready = sem("phi_k_ready")
        x2_ready = sem("x2_ready")
        stats2_ready = sem("stats2_ready")
        mv2_ready = sem("mv2_ready")
        ve2_ready = sem("ve2_ready")
        xn2_ready = sem("xn2_ready")
        kv_own_ready = sem("kv_own_ready")
        den_ready = sem("den_ready")
        rden_ready = sem("rden_ready")
        yn_ready = sem("yn_ready")
        shift_ready = sem("shift_ready")
        xk_ready = sem("xk_ready")
        xr_ready = sem("xr_ready")
        xk_lo_ready = sem("xk_lo_ready")
        xr_lo_ready = sem("xr_lo_ready")
        act_k_ready = sem("act_k_ready")
        act_lo_ready = sem("act_lo_ready")
        yT_lo_ready = sem("yT_lo_ready")
        gated_ready = sem("gated_ready")
        rstd1_ready = sem("rstd1_ready")
        rstd2_ready = sem("rstd2_ready")
        q_par_ready = sem("q_par_ready")
        k_slot_ready = sem("k_slot_ready")
        state_ready = sem("state_ready")
        out_ready = sem("out_ready")

        CONSTS = 11

        def run(eng, step, z_only=False):
            if z_only:
                step(0, -1, True, False, False, False)
            for r in range(FIRST):
                step(0, r, True, True, r >= 1, r >= 2)
            with eng.Fori(0, (MACROS - 1 - FIRST) // UNROLL) as s:
                for r in range(FIRST, FIRST + UNROLL):
                    step(s, r, True, True, True, True)
            last = MACROS // UNROLL - 1
            step(last, 3, False, True, True, True)
            step(last, 4, False, False, True, True)
            step(last, 5, False, False, False, True)

        assert (MACROS - 1 - FIRST) % UNROLL == 0

        block = ctx.enter_context(nc.Block())

        @block.sync
        def _(sp):
            sp.dma_start(x_sb[:, 0], x_m[0]).then_inc(x_in[0], 16)
            weights = (w_q, w_k, w_v, w_o, f_r, f_k, f_v)
            for n, w in enumerate(weights):
                if n == len(EARLY):
                    sp.dma_start(x_sb[:, 1], x_m[1]).then_inc(x_in[1], 16)
                sp.dma_start(w_nat[:, n], w.rearrange("(b p) n -> p b n", p=P)).then_inc(w_in[n], 16)
            with nc.allow_non_contiguous_dma(reason="two short vectors, once"):
                sp.dma_start(mu_r_sb[:, :], mu_r.rearrange("(b p) -> p b", p=P)).then_inc(mu_in, 16)
                sp.dma_start(mu_k_sb[:, :], mu_k.rearrange("(b p) -> p b", p=P)).then_inc(mu_in, 16)
            for m in range(2, 4):
                sp.dma_start(x_sb[:, m], x_m[m]).then_inc(x_in[m], 16)
            with sp.Fori(1, MACROS // 4) as s:
                for r in range(4):
                    sp.wait_ge(x2_ready, 4 * s + r - 3)
                    sp.dma_start(x_sb[:, r], x_m[4 * s + r]).then_inc(x_in[r], 16)
                    sp.wait_ge(out_ready, 4 * s + r - 3)
                    sp.dma_start(out_m[4 * s + r - 4], out_sb[:, r % 2]).then_inc(out_stored[r % 2], 16)
            for m in range(MACROS - 4, MACROS):
                sp.wait_ge(out_ready, m + 1)
                sp.dma_start(out_m[m], out_sb[:, m % 2]).then_inc(out_stored[m % 2], 16)
            for n in range(2):
                sp.wait_ge(out_stored[n], 16 * (MACROS // 2))

        @block.gpsimd
        def _(pool):
            g = nc.gpsimd
            g.memset(ident[:, :], 0.0).then_inc(picks_ready, 1)
            g.memset(diagonals[:, :], 1.0).then_inc(picks_ready, 1)
            g.memset(head_pick[:, :], 1.0).then_inc(picks_ready, 1)
            pool.wait_ge(picks_ready, 3)
            g.affine_select(out=ident[:, :], in_=ident[:, :], compare_op=ALU.not_equal, fill=1.0, base=0,
                            pattern=[[-1, P]], channel_multiplier=1).then_inc(ident_ready, 1)
            g.affine_select(out=diagonals[:, :], in_=diagonals[:, :], compare_op=ALU.is_ge, fill=0.0, base=0,
                            pattern=[[CHUNK, 2], [1, CHUNK]], channel_multiplier=-1).then_inc(picks_ready, 1)
            g.affine_select(out=head_pick[:, :], in_=head_pick[:, :], compare_op=ALU.is_ge, fill=0.0, base=0,
                            pattern=[[-32, 4]], channel_multiplier=1).then_inc(picks_ready, 1)
            pool.wait_ge(picks_ready, 5)
            g.affine_select(out=head_pick[:, :], in_=head_pick[:, :], compare_op=ALU.is_ge, fill=0.0,
                            base=DH - 1, pattern=[[32, 4]], channel_multiplier=-1).then_inc(picks_ready, 1)
            pool.wait_ge(const_ready, CONSTS)

            def step(s, r, Z, A, B, C):
                i, k = 4 * s + r, r % 4
                def add_state(t):
                    pool.wait_ge(kv_own_ready, 2 * i - 1 + t)
                    if ahead(2 * i - 2 + t):
                        pool.wait_ge(state_ready, 2 * i - 2 + t)
                    before = zero_state if (k - 1) % 4 == 0 and t == 0 else state[:, 1 - t]
                    g.tensor_tensor(state[:, t], kv_own[:, t],
                                    before[:, :, 1:2].to_broadcast([P, KB, 2, 4 * VW]),
                                    ALU.add).then_inc(state_ready, 1)

                def next_rstd():
                    pool.wait_ge(ve1_ready, i + 2)
                    g.tensor_tensor(rstd1[:, :], ve1[:, :], minus_half[:, :], ALU.pow).then_inc(rstd1_ready, 1)

                early = isinstance(s, int) and i == 0
                if C:
                    pool.wait_ge(ve2_ready, i - 1)
                    g.tensor_tensor(rstd2[:, :], ve2[:, :], minus_half[:, :], ALU.pow).then_inc(rstd2_ready, 1)

                if B:
                    add_state(0)
                if early:
                    g.memset(k_par[:, :], 0.0).then_inc(v_init, 1)
                    g.memset(v_state[:, :], 0.0).then_inc(v_init, 1)
                    g.memset(v_pair[:, :], 0.0).then_inc(v_init, 1)
                    next_rstd()
                if A:
                    pool.wait_ge(phi_q_ready, i + 1)
                    if ahead(2 * i - 2):
                        pool.wait_ge(pe_y, 2 * i - 2)
                    g.tensor_tensor(
                        q_par[:, k % 2].rearrange("p b g r q -> p (b g) r q"),
                        phi_q[:, :, :].rearrange("p b (g q) -> p (b g) q", q=CHUNK).unsqueeze(2)
                        .to_broadcast([P, 2 * KB * TILES, 2, CHUNK]),
                        par_mask[:, :].unsqueeze(1).unsqueeze(3).to_broadcast([P, 2 * KB * TILES, 2, CHUNK]),
                        ALU.mult).then_inc(q_par_ready, 1)
                if A:
                    pool.wait_ge(phi_k_ready, i + 1)
                    if ahead(2 * i - 2):
                        pool.wait_ge(pe_scores, 2 * i - 2)
                    g.tensor_tensor(
                        k_slot[:, k % 2].rearrange("p b g r q -> p (b g) r q"),
                        phi_k[:, :, :].rearrange("p b (g q) -> p (b g) q", q=CHUNK).unsqueeze(2)
                        .to_broadcast([P, 2 * KB * TILES, 2, CHUNK]),
                        slot_mask[:, :].unsqueeze(1).unsqueeze(3).to_broadcast([P, 2 * KB * TILES, 2, CHUNK]),
                        ALU.mult).then_inc(k_slot_ready, 1)
                if Z and not early:
                    next_rstd()
                if B:
                    add_state(1)
                if C:
                    pool.wait_ge(gated_ready, i - 1)
                    looped = not isinstance(s, int)
                    stores = 2 * s + (r - 2) // 2
                    if ahead(stores) and not (looped and r == FIRST):
                        pool.wait_ge(out_stored[k % 2], 16 * stores)
                    if looped and r == FIRST + UNROLL - 1:
                        pool.wait_ge(out_stored[1 - k % 2], 16 * (2 * s + (r - 1) // 2))
                    g.tensor_tensor(out_sb[:, k % 2], gated[:, :], x2[:, k % 2], ALU.add).then_inc(out_ready, 1)

            run(pool, step, z_only=True)

        @block.scalar
        def _(act):
            a = nc.scalar

            def weights_hi(some):
                for n in some:
                    act.wait_ge(w_turned, n + 1)
                    a.activation(w_hi[:, n], ps_w[n], ACT.Copy, scale=0.5 if n == FV else 1.0).then_inc(w_hi_ready, 1)

            weights_hi(EARLY)

            def step(s, r, Z, A, B, C):
                i, k = 4 * s + r, r % 4
                b = k % 2
                if A:
                    act.wait_ge(pe_xT, i + 1)
                    if ahead(i - 1):
                        act.wait_ge(pe_v, i)
                    a.activation(xT_hi[:, :], ps_xT, ACT.Copy).then_inc(xT_hi_ready, 1)
                if B:
                    act.wait_ge(pe_ktok, i)
                    if ahead(2 * i - 4):
                        act.wait_ge(pe_kv, 2 * i - 4)
                    for par in range(2):
                        a.activation(
                            k_par[:, 1 - b, par].rearrange("p t (g r d) -> p (t g) r d", r=2, d=DH)[:, :, par],
                            ps_ktok.rearrange("p t (g r d) -> p (t g) r d", r=2, d=DH)[:, :, par],
                            ACT.Copy).then_inc(k_par_ready, 1)
                if A:
                    for ps, relu, exp, done, phi, signal in (
                            (ps_q, q_relu, q_exp, pe_q, phi_q_ready, q_raw_ready),
                            (ps_k, k_relu, k_exp, pe_k, phi_k_ready, k_raw_ready)):
                        act.wait_ge(done, i + 1)
                        if ahead(i):
                            act.wait_ge(phi, i)
                        a.activation(relu[:, :], ps, ACT.Relu).then_inc(signal, 1)
                        a.activation(exp[:, :], ps, ACT.Exp).then_inc(signal, 1)
                if C:
                    act.wait_ge(pe_x2T, i - 1)
                    a.activation(x2T[:, b, :, 1:1 + MACRO], feat[0], ACT.Copy).then_inc(x2T_ready, 1)
                    first = (k - 2) % 4 == 0
                    if ahead(2 * i - 4) and not first:
                        act.wait_ge(x2T_ready, 2 * i - 4)
                    a.activation(x2T[:, b, :, 0:1], zero_col[:, :] if first else x2T[:, 1 - b, :, MACRO:1 + MACRO],
                                 ACT.Copy).then_inc(x2T_ready, 1)
                    for src, hi, ready, used, signal in ((xk, xk_hi, xk_ready, pe_fk, xk_hi_ready),
                                                         (xr, xr_hi, xr_ready, pe_r, xr_hi_ready)):
                        act.wait_ge(ready, 2 * i - 2)
                        if ahead(i - 2):
                            act.wait_ge(used, i - 2)
                        a.activation(hi[:, :], src[:, :], ACT.Copy).then_inc(signal, 1)
                if isinstance(s, int) and i == 0:
                    weights_hi(LATE)
                if A:
                    act.wait_ge(pe_v, i + 1)
                    if isinstance(s, int) and i == 0:
                        act.wait_ge(v_init, 3 + 12)
                        act.wait_ge(const_ready, CONSTS)
                    if ahead(2 * i - 2):
                        act.wait_ge(pe_y, 2 * i - 2)
                    heads = ps_v.rearrange("p t (h d) -> p t h d", d=DH)
                    a.activation(v_state[:, b, :, 1, :, 0:DH], heads, ACT.Copy).then_inc(v_ready, 1)
                    a.activation(v_state[0:CHUNK, b, :, 0, :, 0:DH], heads[0:CHUNK], ACT.Copy).then_inc(v_ready, 1)
                    pairs = ps_v.rearrange("p t (g s r d) -> p (t g) s r d", s=2, r=2, d=DH)
                    for c in range(2):
                        for p2 in range(2):
                            a.activation(
                                v_pair[p2 * CHUNK:(p2 + 1) * CHUNK, b, c].rearrange(
                                    "p t g r s w -> p (t g) r s w")[:, :, :, p2, 0:DH],
                                pairs[c * CHUNK:(c + 1) * CHUNK, :, p2], ACT.Copy).then_inc(v_ready, 1)
                if C:
                    act.wait_ge(pe_fk, i - 1)
                    if ahead(i - 2):
                        act.wait_ge(act_k_ready, i - 2)
                    a.activation(relu_k[:, :], ps_fk, ACT.Relu).then_inc(relu_k_ready, 1)
                    act.wait_ge(relu_k_ready, i - 1)
                    if ahead(i - 2):
                        act.wait_ge(pe_fo, i - 2)
                    a.activation(act_hi[:, :], relu_k[:, :], ACT.Square).then_inc(act_hi_ready, 1)
                if C:
                    act.wait_ge(pe_r, i - 1)
                    if ahead(i - 2):
                        act.wait_ge(gated_ready, i - 2)
                    a.activation(tanh_r[:, :], ps_r, ACT.Tanh, scale=0.5).then_inc(tanh_ready, 1)
                if B:
                    act.wait_ge(pe_yT, i)
                    if ahead(i - 1):
                        act.wait_ge(pe_wo, i - 1)
                    a.activation(yT_hi[:, :].rearrange("p r (g q) -> p g r q", q=CHUNK),
                                 bank[0][:, :].rearrange("p (g r q) -> p g r q", r=2, q=CHUNK),
                                 ACT.Copy).then_inc(yT_hi_ready, 1)

            run(act, step)

        @block.vector
        def _(dve):
            v = nc.vector
            v.memset(minus_half[:, :], -0.5).then_inc(const_ready, 1)
            v.memset(zero_state[:, :], 0.0).then_inc(const_ready, 1)
            v.memset(zero_col[:, :], 0.0).then_inc(const_ready, 1)
            v.memset(slot_mask[:, :], 0.0).then_inc(masks_ready, 1)
            v.memset(pair_mask[:, :], 0.0).then_inc(masks_ready, 1)
            dve.wait_ge(masks_ready, 2)
            for g in range(4):
                v.memset(slot_mask[32 * g:32 * g + 32, g % 2:g % 2 + 1], 1.0).then_inc(const_ready, 1)
            for g in range(4):
                v.memset(pair_mask[32 * g:32 * g + 32, g:g + 1], 1.0).then_inc(masks_ready, 1)
            dve.wait_ge(picks_ready, 6)
            v.tensor_reduce(par_mask[:, 0:1], head_pick[:, :], mybir.AxisListType.X, ALU.add).then_inc(const_ready, 1)
            for half in range(2):
                rows = slice(half * CHUNK, (half + 1) * CHUNK)
                v.tensor_copy(causal[rows, :], diagonals[rows, half]).then_inc(const_ready, 1)
            dve.wait_ge(const_ready, CONSTS - 1)
            v.tensor_scalar(par_mask[:, 1:2], par_mask[:, 0:1], -1.0, 1.0, ALU.mult, ALU.add).then_inc(const_ready, 1)

            def weights_lo(some):
                for n in some:
                    dve.wait_ge(w_hi_ready, n + 1)
                    v.scalar_tensor_tensor(out=w_lo[:, n], in0=ps_w[n], scalar=0.5 if n == FV else 1.0,
                                           in1=w_hi[:, n].bitcast(F32), op0=ALU.mult,
                                           op1=ALU.subtract).then_inc(w_ready, 1)

            def sort_w_o():
                dve.wait_ge(w_in[WO], 16)
                for d in range(KB):
                    v.tensor_copy(w_o_sorted[:, d], w_nat[:, WO, d].rearrange("p (g r v) -> p r g v", r=2, v=DH))\
                     .then_inc(w_o_ready, 1)

            def ones_columns():
                dve.wait_ge(v_init, 3)
                for n in range(2):
                    v.memset(v_state[:, n, :, 1, :, DH:VW], 1.0).then_inc(v_init, 1)
                    v.memset(v_state[0:CHUNK, n, :, 0, :, DH:VW], 1.0).then_inc(v_init, 1)
                    for p2 in range(2):
                        for c in range(2):
                            v.memset(v_pair[p2 * CHUNK:(p2 + 1) * CHUNK, n, c, :, :, :, p2, DH:VW]
                                     .rearrange("p t g r w -> p (t g r) w"), 1.0).then_inc(v_init, 1)

            def step(s, r, Z, A, B, C):
                i, k = 4 * s + r, r % 4
                b = k % 2

                def mask_scores(t):
                    dve.wait_ge(pe_scores, 2 * i - 1 + t)
                    if ahead(2 * i - 3 + t):
                        dve.wait_ge(pe_y, 2 * i - 3 + t)
                    v.tensor_tensor(probs[:, t].rearrange("p a c b r q -> p (a c b r) q"),
                                    bank_scores[:, :, :].rearrange("p a (c q) -> p (a c) q", q=CHUNK),
                                    causal[:, :].unsqueeze(1).to_broadcast([P, HEADS, CHUNK]),
                                    ALU.mult).then_inc(probs_ready, 1)

                def normalise(t):
                    dve.wait_ge(pe_y, 2 * i - 1 + t)
                    v.tensor_scalar(den[:, t], ps_y[:, :, DH], DEN_MIN, None, ALU.max).then_inc(den_ready, 1)
                    dve.wait_ge(den_ready, 2 * i - 1 + t)
                    v.reciprocal(rden[:, t], den[:, t]).then_inc(rden_ready, 1)
                    dve.wait_ge(rden_ready, 2 * i - 1 + t)
                    if ahead(i - 1):
                        dve.wait_ge(pe_yT, i - 1)
                    v.tensor_tensor(yn[:, t], ps_y[:, :, 0:DH],
                                    rden[:, t].unsqueeze(2).to_broadcast([P, HEADS, DH]),
                                    ALU.mult).then_inc(yn_ready, 1)

                def own_pairs(t):
                    dve.wait_ge(pe_kv, 2 * i - 1 + t)
                    if t == 0:
                        dve.wait_ge(masks_ready, 6)
                    if ahead(2 * i - 3 + t):
                        dve.wait_ge(state_ready, 2 * i - 3 + t)
                    v.tensor_tensor(kv_own[:, t].rearrange("p b c (g w) -> p (b c) g w", g=4),
                                    ps_kv.rearrange("p b (c w) -> p (b c) w", c=2).unsqueeze(2)
                                    .to_broadcast([P, 2 * KB, 4, VW]),
                                    pair_mask[:, :].unsqueeze(1).unsqueeze(3).to_broadcast([P, 2 * KB, 4, VW]),
                                    ALU.mult).then_inc(kv_own_ready, 1)

                def statistics(src, stats, signal):
                    for t in range(TILES):
                        v.bn_stats(stats[:, t], src[:, t]).then_inc(signal, 1)

                def moments(stats, mv, ve, n, mv_sem, ve_sem):
                    for t in range(TILES):
                        v.bn_aggr(mv[:, t], stats[:, t]).then_inc(mv_sem, 1)
                    dve.wait_ge(mv_sem, 2 * n)
                    v.tensor_scalar(ve[:, :], mv[:, :, 1], LN_EPS, None, ALU.add).then_inc(ve_sem, 1)

                def next_statistics():
                    dve.wait_ge(x_in[(k + 1) % 4], 16 * (s + (r + 1) // 4 + 1))
                    statistics(x_sb[:, (k + 1) % 4], stats1, stats1_ready)
                    dve.wait_ge(stats1_ready, 2 * i + 4)

                early = isinstance(s, int) and i == 0
                if A:
                    if early:
                        weights_lo(EARLY)
                    dve.wait_ge(xT_hi_ready, i + 1)
                    v.tensor_tensor(xT_lo[:, :], ps_xT, xT_hi[:, :].bitcast(F32), ALU.subtract).then_inc(xT_lo_ready, 1)
                if early:
                    sort_w_o()
                    next_statistics()
                    moments(stats1, mv1, ve1, i + 2, mv1_ready, ve1_ready)
                    ones_columns()
                if C:
                    dve.wait_ge(pe_wo, i - 1)
                    v.tensor_tensor(x2[:, b], x_sb[:, (k - 2) % 4], ps_wo, ALU.add).then_inc(x2_ready, 1)
                    dve.wait_ge(x2_ready, i - 1)
                    statistics(x2[:, b], stats2, stats2_ready)
                if C:
                    dve.wait_ge(stats2_ready, 2 * i - 2)
                    v.memset(wait_carrier[:, :], 0.0)
                    moments(stats2, mv2, ve2, i - 1, mv2_ready, ve2_ready)
                if B:
                    mask_scores(0)
                if C:
                    dve.wait_ge(rstd2_ready, i - 1)
                    if ahead(i - 2):
                        dve.wait_ge(pe_x2T, i - 2)
                    for t in range(TILES):
                        v.tensor_scalar(xn2[:, t], x2[:, b, t], mv2[:, t, 0:1], rstd2[:, t:t + 1],
                                        ALU.subtract, ALU.mult).then_inc(xn2_ready, 1)
                if B:
                    own_pairs(0)
                if A:
                    dve.wait_ge(q_raw_ready, 2 * i + 2)
                    if ahead(i):
                        dve.wait_ge(q_par_ready, i)
                    v.scalar_tensor_tensor(out=phi_q[:, :], in0=q_exp[:, :], scalar=1.0, in1=q_relu[:, :],
                                           op0=ALU.min, op1=ALU.add).then_inc(phi_q_ready, 1)
                if Z and not early:
                    next_statistics()
                if A:
                    dve.wait_ge(k_raw_ready, 2 * i + 2)
                    if ahead(i):
                        dve.wait_ge(k_slot_ready, i)
                        dve.wait_ge(pe_ktok, i)
                    v.scalar_tensor_tensor(out=phi_k[:, :], in0=k_exp[:, :], scalar=1.0, in1=k_relu[:, :],
                                           op0=ALU.min, op1=ALU.add).then_inc(phi_k_ready, 1)
                if Z and not early:
                    moments(stats1, mv1, ve1, i + 2, mv1_ready, ve1_ready)
                if C:
                    dve.wait_ge(x2T_ready, 2 * i - 2)
                    v.tensor_tensor(shift[:, :], x2T[:, b, :, 1:1 + MACRO], x2T[:, b, :, 0:MACRO],
                                    ALU.subtract).then_inc(shift_ready, 1)
                    dve.wait_ge(shift_ready, i - 1)
                    for mu, mix, read, signal in ((mu_k_sb, xk, xk_hi_ready, xk_ready),
                                                  (mu_r_sb, xr, xr_hi_ready, xr_ready)):
                        if ahead(i - 2):
                            dve.wait_ge(read, i - 2)
                        for c in range(KB):
                            v.scalar_tensor_tensor(out=mix[:, c], in0=shift[:, c], scalar=mu[:, c:c + 1],
                                                   in1=x2T[:, b, c, 0:MACRO], op0=ALU.mult,
                                                   op1=ALU.add).then_inc(signal, 1)
                if C:
                    dve.wait_ge(xk_ready, 2 * i - 2)
                    dve.wait_ge(xk_hi_ready, i - 1)
                    v.tensor_tensor(xk_lo[:, :], xk[:, :], xk_hi[:, :].bitcast(F32),
                                    ALU.subtract).then_inc(xk_lo_ready, 1)
                if B:
                    normalise(0)
                    mask_scores(1)
                    own_pairs(1)
                if C:
                    dve.wait_ge(xr_ready, 2 * i - 2)
                    dve.wait_ge(xr_hi_ready, i - 1)
                    v.tensor_tensor(xr_lo[:, :], xr[:, :], xr_hi[:, :].bitcast(F32),
                                    ALU.subtract).then_inc(xr_lo_ready, 1)
                if early:
                    weights_lo(LATE)
                    dve.wait_ge(mu_in, 32)
                if Z:
                    dve.wait_ge(rstd1_ready, i + 2)
                    if ahead(i + 1):
                        dve.wait_ge(pe_xT, i + 1)
                    for t in range(TILES):
                        v.tensor_scalar(xn1[:, t], x_sb[:, (k + 1) % 4, t], mv1[:, t, 0:1], rstd1[:, t:t + 1],
                                        ALU.subtract, ALU.mult).then_inc(xn1_ready, 1)
                if C:
                    dve.wait_ge(relu_k_ready, i - 1)
                    v.tensor_tensor(act_k[:, :], relu_k[:, :], relu_k[:, :], ALU.mult).then_inc(act_k_ready, 1)
                if B:
                    normalise(1)
                if C:
                    dve.wait_ge(act_k_ready, i - 1)
                    dve.wait_ge(act_hi_ready, i - 1)
                    v.tensor_tensor(act_lo[:, :], act_k[:, :], act_hi[:, :].bitcast(F32),
                                    ALU.subtract).then_inc(act_lo_ready, 1)
                if B:
                    dve.wait_ge(yT_hi_ready, i)
                    v.tensor_tensor(yT_lo[:, :].rearrange("p r (g q) -> p g r q", q=CHUNK),
                                    bank[0][:, :].rearrange("p (g r q) -> p g r q", r=2, q=CHUNK),
                                    yT_hi[:, :].bitcast(F32).rearrange("p r (g q) -> p g r q", q=CHUNK),
                                    ALU.subtract).then_inc(yT_lo_ready, 1)
                if C:
                    dve.wait_ge(pe_fo, i - 1)
                    dve.wait_ge(tanh_ready, i - 1)
                    if ahead(i - 2):
                        dve.wait_ge(out_ready, i - 2)
                    v.scalar_tensor_tensor(out=gated[:, :].rearrange("p t n -> p (t n)"),
                                           in0=tanh_r[:, :].rearrange("p t n -> p (t n)"), scalar=1.0,
                                           in1=bank_kv[:, :], op0=ALU.add, op1=ALU.mult).then_inc(gated_ready, 1)

            run(dve, step, z_only=True)

        @block.tensor
        def _(pe):
            mm, turn = nc.tensor.matmul, nc.tensor.transpose

            def turn_weights(some):
                for n in some:
                    if n == WO:
                        pe.wait_ge(w_o_ready, KB)
                    else:
                        pe.wait_ge(w_in[n], 16)
                    for c in range(KB):
                        for d in range(KB):
                            if n == WO:
                                src = w_o_sorted[:, d, c].rearrange("p g v -> p (g v)")
                            else:
                                src = w_nat[:, n, d, c * P:(c + 1) * P]
                            last = turn(ps_w[n][:, c, d * P:(d + 1) * P], src, ident[:, :])
                    last.then_inc(w_turned, 1)

            pe.wait_ge(ident_ready, 1)
            turn_weights(EARLY)

            def by_feature(ps, n, hi, lo):
                for m in range(KB):
                    parts = [(w, o, c) for w, o in ((w_hi, hi), (w_hi, lo), (w_lo, hi)) for c in range(KB)]
                    for j, (w, o, c) in enumerate(parts):
                        last = mm(ps[:, m], w[:, n, c, m * P:(m + 1) * P], o[:, c],
                                  start=j == 0, stop=j == len(parts) - 1)
                return last

            def by_token(ps, n, hi, lo):
                for t in range(TILES):
                    parts = [(o, w, c) for o, w in ((hi, w_hi), (hi, w_lo), (lo, w_hi)) for c in range(KB)]
                    for j, (o, w, c) in enumerate(parts):
                        last = mm(ps[:, t], o[:, c, t * P:(t + 1) * P], w[:, n, c],
                                  start=j == 0, stop=j == len(parts) - 1)
                return last

            def step(s, r, Z, A, B, C):
                i, k = 4 * s + r, r % 4
                a_buf, b_buf = k % 2, (k - 1) % 2

                def scores(t):
                    for c in range(2):
                        for blk in range(KB):
                            for hi2 in range(2):
                                rows = slice(hi2 * CHUNK, (hi2 + 1) * CHUNK)
                                at = (c * KB + blk) * P
                                last = mm(bank_scores[:, hi2, at:at + P],
                                          k_slot[rows, b_buf, blk, 2 * t + c].rearrange("p r q -> p (r q)"),
                                          q_par[rows, b_buf, blk, 2 * t + c].rearrange("p r q -> p (r q)"),
                                          start=True, stop=True)
                    last.then_inc(pe_scores, 1)

                def state_products(t):
                    heads = v_state[:, b_buf, t].rearrange("p c (b g r) w -> p b g r c w", b=KB, r=2)
                    for blk in range(KB):
                        for par in range(2):
                            for g in range(4):
                                at = blk * P + 32 * g
                                last = mm(ps_kv[32 * g:32 * g + 32, blk], k_par[:, b_buf, par, t, at:at + 32],
                                          heads[:, blk, g, par], start=par == 0, stop=par == 1)
                    last.then_inc(pe_kv, 1)

                def attend(t):
                    pe.wait_ge(probs_ready, 2 * i - 1 + t)
                    for c in range(2):
                        for quad in range(4):
                            blk, hi2 = quad // 2, quad % 2
                            for par in range(2):
                                g = c * PAIRS + 2 * quad
                                mm(ps_y[par * CHUNK:(par + 1) * CHUNK, g:g + 2],
                                   probs[:, t, hi2, c, blk, par],
                                   v_pair[:, b_buf, c, t, quad, par],
                                   start=c == 0 and quad == 0, stop=False, skip_group_check=True)
                    pe.wait_ge(state_ready, 2 * i - 1 + t)
                    before = state[:, 1 - t]
                    first = (k - 1) % 4 == 0 and t == 0
                    for c in range(1 if first else 0, 2):
                        for blk in range(KB):
                            g = c * PAIRS + 4 * blk
                            prefix = before[:, blk, 1] if c == 0 else state[:, t, blk, 0]
                            last = mm(ps_y[:, g:g + 4],
                                      q_par[:, b_buf, blk, 2 * t + c].rearrange("p r q -> p (r q)"),
                                      prefix, start=False, stop=True, skip_group_check=True)
                    last.then_inc(pe_y, 1)

                if B:
                    pe.wait_ge(phi_k_ready, i)
                    pe.wait_ge(v_ready, 6 * i)
                    for t in range(TILES):
                        for c in range(KB):
                            last = turn(ps_ktok[:, t, c * P:(c + 1) * P], phi_k[:, c, t * P:(t + 1) * P], ident[:, :])
                    last.then_inc(pe_ktok, 1)
                if A:
                    pe.wait_ge(xn1_ready, 2 * i + 2)
                    if ahead(i - 1):
                        pe.wait_ge(yT_lo_ready, i - 1)
                    for t in range(TILES):
                        for c in range(KB):
                            last = turn(ps_xT[:, c, t * P:(t + 1) * P], xn1[:, t, c * P:(c + 1) * P], ident[:, :])
                    last.then_inc(pe_xT, 1)
                if isinstance(s, int) and i == 0:
                    pe.wait_ge(w_ready, len(EARLY))
                if isinstance(s, int) and i == 1:
                    pe.wait_ge(w_ready, NW)
                if C:
                    pe.wait_ge(yT_lo_ready, i - 1)
                    pe.wait_ge(yn_ready, 2 * i - 2)
                    by_token(ps_wo, WO, yT_hi, yT_lo).then_inc(pe_wo, 1)
                if B:
                    pe.wait_ge(q_par_ready, i)
                    pe.wait_ge(k_slot_ready, i)
                    if ahead(2 * i - 2):
                        pe.wait_ge(probs_ready, 2 * i - 2)
                    scores(0)
                if A:
                    pe.wait_ge(xT_lo_ready, i + 1)
                    if ahead(i - 2):
                        pe.wait_ge(relu_k_ready, i - 2)
                    by_feature(ps_q, WQ, xT_hi, xT_lo).then_inc(pe_q, 1)
                if B:
                    pe.wait_ge(k_par_ready, 2 * i)
                    if ahead(i - 2):
                        pe.wait_ge(gated_ready, i - 2)
                    state_products(0)
                if A:
                    if ahead(i - 2):
                        pe.wait_ge(tanh_ready, i - 2)
                    by_feature(ps_k, WK, xT_hi, xT_lo).then_inc(pe_k, 1)
                if isinstance(s, int) and i == 0:
                    turn_weights(LATE)
                if C:
                    pe.wait_ge(xn2_ready, 2 * i - 2)
                    if A:
                        pe.wait_ge(xT_lo_ready, i + 1)
                    for t in range(TILES):
                        for c in range(KB):
                            last = turn(feat[0][:, c, t * P:(t + 1) * P], xn2[:, t, c * P:(c + 1) * P], ident[:, :])
                    last.then_inc(pe_x2T, 1)
                if B:
                    pe.wait_ge(probs_ready, 2 * i - 1)
                    scores(1)
                    if ahead(i - 1):
                        pe.wait_ge(x2_ready, i - 1)
                    attend(0)
                if A:
                    if ahead(2 * i):
                        pe.wait_ge(k_par_ready, 2 * i)
                    by_token(ps_v, WV, xT_hi, xT_lo).then_inc(pe_v, 1)
                if B:
                    pe.wait_ge(kv_own_ready, 2 * i - 1)
                    state_products(1)
                if C:
                    pe.wait_ge(xk_lo_ready, i - 1)
                    if A:
                        pe.wait_ge(q_raw_ready, 2 * i + 2)
                    by_feature(ps_fk, FK, xk_hi, xk_lo).then_inc(pe_fk, 1)
                if B:
                    pe.wait_ge(yn_ready, 2 * i - 1)
                    attend(1)
                if C:
                    pe.wait_ge(xr_lo_ready, i - 1)
                    if A:
                        pe.wait_ge(k_raw_ready, 2 * i + 2)
                    by_token(ps_r, FR, xr_hi, xr_lo).then_inc(pe_r, 1)
                if B:
                    pe.wait_ge(yn_ready, 2 * i)
                    if C:
                        pe.wait_ge(x2T_ready, 2 * i - 2)
                    for t in range(TILES):
                        for c in range(2):
                            last = turn(bank[0][:, (2 * t + c) * P:(2 * t + c + 1) * P],
                                        yn[:, t, c * PAIRS:(c + 1) * PAIRS].rearrange("p g v -> p (g v)"),
                                        ident[:, :])
                    last.then_inc(pe_yT, 1)
                if C:
                    pe.wait_ge(act_lo_ready, i - 1)
                    if B:
                        pe.wait_ge(kv_own_ready, 2 * i)
                    by_token(ps_fo, FV, act_hi, act_lo).then_inc(pe_fo, 1)

            run(pe, step)


_INS = ["L0_attn_x", "L0_attn_W_q", "L0_attn_W_k", "L0_attn_W_v", "L0_attn_W_o",
        "L0_ffn_W_r", "L0_ffn_W_k", "L0_ffn_W_v", "L0_ffn_mu_r", "L0_ffn_mu_k"]


def kernel(**inputs):
    import numpy as _np
    import concourse.bacc as _bacc
    from concourse import mybir as _mybir
    from concourse.bass_utils import run_bass_kernel_spmd as _run

    nc = _bacc.Bacc("TRN2", target_bir_lowering=False, num_devices=1)
    arrays, args = {}, []
    for name in _INS:
        a = _np.ascontiguousarray(inputs[name])
        arrays[f"in_{name}_dram"] = a
        args.append(nc.dram_tensor(f"in_{name}_dram", a.shape, _mybir.dt.from_np(a.dtype), kind="ExternalInput").ap())
    shape = inputs["L0_attn_x"].shape
    args.append(nc.dram_tensor("out_dram", shape, _mybir.dt.float32, kind="ExternalOutput").ap())
    build(nc, *args)
    r = _run(nc, [arrays], core_ids=[0])
    return r.results[0]["out_dram"]
```
